# Optimizing a Trainium2 kernel written in Bass

```python
import numpy as np
import jax
import jax.numpy as jnp

def _softmax(x, axis=-1):
    return jax.nn.softmax(x, axis=axis)

def _gelu(x):
    return jax.nn.gelu(x, approximate=True)

def _silu(x):
    return jax.nn.silu(x)

def _sigmoid(x):
    return jax.nn.sigmoid(x)

def _layernorm(x, axis=-1, eps=1e-05):
    m = jnp.mean(x, axis=axis, keepdims=True)
    v = jnp.var(x, axis=axis, keepdims=True)
    return (x - m) / jnp.sqrt(v + eps)

def _scatter_add(tgt, idx, src, axis=0):
    return tgt.at[idx].add(src)

def _segment_sum(src, seg, n):
    return jax.ops.segment_sum(src, seg, n)
kernel_name = 'mk_adaln_ffn_d1_seqx_r8_5aa765'

def setup_inputs(seed: int=0):
    np.random.seed(seed)
    _w = jnp.asarray

    def _rec_inputs():
        import jax
        import jax.numpy as jnp
        _rk = jax.random.key(seed)
        x = -0.000125 + 0.9999 * jax.random.normal(jax.random.fold_in(_rk, 1), (128, 32, 512), jnp.float32)
        _lenS = 32 - jax.random.randint(jax.random.fold_in(_rk, 7), (128,), 0, max(1, 32 // 4) + 1, jnp.int32)
        _lenS2 = 32 - jax.random.randint(jax.random.fold_in(_rk, 8), (128,), 0, max(1, 32 // 4) + 1, jnp.int32)
        cond_128 = 0.0061147 + 1.02565 * jax.random.normal(jax.random.fold_in(_rk, 11), (128, 128), jnp.float32)
        fside_S_0 = -0.022604 + 0.987366 * jax.random.normal(jax.random.fold_in(_rk, 12), (32,), jnp.float32)
        return (x, cond_128, fside_S_0)
    x, cond_128, fside_S_0 = _rec_inputs()

    def _L0_cond_setup():
        import jax, jax.numpy as jnp
        import numpy as np
        from jax import lax
        N, C_IN, L = (32, 32, 512)
        C_OUT, K, GROUPS = (32, 9, 4)
        C_DIM, PAD, STRIDE = (128, 4, 1)
        key = jax.random.key(seed)
        k1, k2, k3, k4, k5 = jax.random.split(key, 5)
        x = jax.random.normal(k1, (N, C_IN, L), dtype=jnp.float32)
        c = jax.random.normal(k2, (N, C_DIM), dtype=jnp.float32)
        weight = jax.random.normal(k3, (C_OUT, C_IN // GROUPS, K), dtype=jnp.float32)
        c_weight = jax.random.normal(k4, (C_OUT, C_DIM), dtype=jnp.float32)
        bias = jax.random.normal(k5, (C_OUT,), dtype=jnp.float32)
        return {'x': x, 'c': c, 'weight': weight, 'c_weight': c_weight, 'bias': bias}
    _L0_cond_all = _L0_cond_setup()
    _L0_cond_in = {k: v for k, v in _L0_cond_all.items() if k in ('weight', 'c_weight')}
    del _L0_cond_all

    def _L0_ffn_setup():
        import jax, jax.numpy as jnp
        import numpy as np
        B_, S, D_IN, D_OUT = (4, 256, 512, 512)
        N, RANK, ALPHA = (8, 16, 32)
        SCALE = ALPHA / RANK
        key = jax.random.key(seed)
        kx, ka, kb, kw, kbias = jax.random.split(key, 5)
        x = jax.random.normal(kx, (B_, S, D_IN), dtype=jnp.float32)
        lora_A = jax.random.normal(ka, (N, RANK, D_IN), dtype=jnp.float32) * (1.0 / np.sqrt(D_IN))
        lora_B = jax.random.normal(kb, (N, D_OUT, RANK), dtype=jnp.float32) * (1.0 / np.sqrt(RANK))
        W = jax.random.normal(kw, (D_OUT, D_IN), dtype=jnp.float32) * (1.0 / np.sqrt(D_IN))
        bias = jax.random.normal(kbias, (D_OUT,), dtype=jnp.float32) * 0.01
        lora_weights = jnp.full((N,), 1.0 / N, dtype=jnp.float32)
        return {'x': x, 'lora_A': lora_A, 'lora_B': lora_B, 'W': W, 'bias': bias, 'lora_weights': lora_weights}
    _L0_ffn_all = _L0_ffn_setup()
    _L0_ffn_in = {k: v for k, v in _L0_ffn_all.items() if k in ('lora_A', 'lora_B', 'W', 'bias', 'lora_weights')}
    del _L0_ffn_all
    return {'x': x, 'cond_128': cond_128, 'fside_S_0': fside_S_0, 'L0_cond_weight': _L0_cond_in['weight'], 'L0_cond_c_weight': _L0_cond_in['c_weight'], 'L0_ffn_lora_A': _L0_ffn_in['lora_A'], 'L0_ffn_lora_B': _L0_ffn_in['lora_B'], 'L0_ffn_W': _L0_ffn_in['W'], 'L0_ffn_bias': _L0_ffn_in['bias'], 'L0_ffn_lora_weights': _L0_ffn_in['lora_weights']}

def reference(x, cond_128, fside_S_0, L0_cond_weight, L0_cond_c_weight, L0_ffn_lora_A, L0_ffn_lora_B, L0_ffn_W, L0_ffn_bias, L0_ffn_lora_weights):
    import jax
    import jax.numpy as jnp

    def _L0_cond_ref(x, c, weight, c_weight, bias):
        import jax, jax.numpy as jnp
        import numpy as np
        from jax import lax
        N, C_IN, L = (32, 32, 512)
        C_OUT, K, GROUPS = (32, 9, 4)
        C_DIM, PAD, STRIDE = (128, 4, 1)
        out = lax.conv_general_dilated(x, weight, window_strides=(STRIDE,), padding=[(PAD, PAD)], dimension_numbers=('NCH', 'OIH', 'NCH'), feature_group_count=GROUPS)
        ctx = jnp.einsum('nd,od->no', c, c_weight)
        out = out + ctx[:, :, None] + bias[None, :, None]
        return out

    def _L0_ffn_ref(x, lora_A, lora_B, W, bias, lora_weights):
        import jax, jax.numpy as jnp
        import numpy as np
        B_, S, D_IN, D_OUT = (4, 256, 512, 512)
        N, RANK, ALPHA = (8, 16, 32)
        SCALE = ALPHA / RANK
        h = jnp.einsum('bsd,nrd->nbsr', x, lora_A)
        coef = (SCALE * lora_weights)[:, None, None]
        lora_out = jnp.einsum('nbsr,nor->bso', h, lora_B * coef)
        base = jnp.einsum('bsd,od->bso', x, W) + bias
        return base + lora_out
    x = x + _L0_ffn_ref(_L0_cond_ref(x, cond_128, L0_cond_weight, L0_cond_c_weight, fside_S_0), L0_ffn_lora_A, L0_ffn_lora_B, L0_ffn_W, L0_ffn_bias, L0_ffn_lora_weights)
    return x

_drawn_inputs = setup_inputs


def setup_inputs(seed=0):
    import zlib

    import numpy as np

    out = dict(_drawn_inputs(seed))
    spreads = {'L0_ffn_lora_weights': (0.125, 0.2)}
    factors = {'L0_ffn_bias': 64.0}
    for name, (base, spread) in spreads.items():
        noise = np.random.default_rng([zlib.crc32(name.encode()), seed]).standard_normal(out[name].shape)
        drawn = base * np.exp(spread * noise) if base else spread * noise
        out[name] = jnp.asarray(drawn.astype(out[name].dtype))
    for name, factor in factors.items():
        out[name] = (out[name] * factor).astype(out[name].dtype)
    return out
```

```python
from contextlib import ExitStack

import concourse.bass as bass
from concourse import mybir

ALU = mybir.AluOpType
ACT = mybir.ActivationFunctionType
F32 = mybir.dt.float32
F32R = mybir.dt.float32r

P = 128


def adaln_ffn(
    nc: bass.Bass,
    x: bass.AP,
    cond: bass.AP,
    chan_bias: bass.AP,
    conv_w: bass.AP,
    ctx_w: bass.AP,
    lora_a: bass.AP,
    lora_b: bass.AP,
    ffn_w: bass.AP,
    ffn_bias: bass.AP,
    lora_weights: bass.AP,
    out: bass.AP,
):
    N, C, L = x.shape
    OUT_CH, CG, TAPS = conv_w.shape
    GROUPS = C // CG
    NL, RANK, _ = lora_a.shape
    M = ffn_w.shape[0]
    LORA_SCALE = 32.0 / RANK
    S = P // CG
    PAD = TAPS // 2
    J = S + TAPS - 1
    CHUNK = 512 // CG
    Q = L // CHUNK
    TPC = CHUNK // S
    TILES = L // S
    KT = L // P
    MT = M // P
    RING = 4
    HALF = L // 2
    assert N == P and OUT_CH == C and NL * RANK == P and Q == CG and Q % RING == 0 and M == 512

    with ExitStack() as ctx:
        def sb(name, shape, dt=F32):
            return ctx.enter_context(nc.sbuf_tensor(name, shape, dt))

        def ps(name, shape):
            return ctx.enter_context(nc.psum_tensor(name, shape, F32))

        def sem(name):
            return ctx.enter_context(nc.semaphore(name))

        ident = sb("ident", [P, P])
        xres = sb("xres", [P, C, L])
        xtile = sb("xtile", [P, RING, TPC, CG * S])
        xt_hi = sb("xt_hi", [P, RING, TPC * P], F32R)
        xt_lo = sb("xt_lo", [P, RING, TPC * P], F32R)
        conv = sb("conv", [P, CG, L])
        ct_hi = sb("ct_hi", [P, CG, KT * P], F32R)
        ct_lo = sb("ct_lo", [P, CG, KT * P], F32R)
        wt_hi = sb("wt_hi", [P, KT, M], F32R)
        wt_lo = sb("wt_lo", [P, KT, M], F32R)
        toep_rev = sb("toep_rev", [P, GROUPS, CG, J])
        toep_hi = sb("toep_hi", [P, GROUPS, J, CG], F32R)
        toep_lo = sb("toep_lo", [P, GROUPS, J, CG], F32R)
        w_nat = sb("w_nat", [P, MT, L])
        a_nat = sb("a_nat", [P, L])
        b_nat = sb("b_nat", [P, NL, MT, RANK])
        b_col = sb("b_col", [P, MT, NL * RANK])
        bt = sb("bt", [P, M])
        lw_col = sb("lw_col", [P, 1])
        cond_nat = sb("cond_nat", [P, P])
        ctxw_nat = sb("ctxw_nat", [C, P])
        cond_t = sb("cond_t", [P, P + C])
        chan_bias_rows = sb("chan_bias_rows", [P, C])
        row_bias = sb("row_bias", [P, C])
        ffn_bias_rows = sb("ffn_bias_rows", [P, M])

        ps_xt = ps("ps_xt", [P, 2, 512])
        ps_conv = ps("ps_conv", [P, 2, 512])
        ps_ct = ps("ps_ct", [P, 2, 512])
        ps_y = ps("ps_y", [P, 2, 512])

        x0_in = [sem(f"x0_in{i}") for i in range(4)]
        x_in = sem("x_in")
        toep_zero = sem("toep_zero")
        toep_in = sem("toep_in")
        w_in = sem("w_in")
        a_in = sem("a_in")
        b_in = sem("b_in")
        lw_in = sem("lw_in")
        cond_in = sem("cond_in")
        chan_bias_in = sem("chan_bias_in")
        ffn_bias_in = sem("ffn_bias_in")
        ident_zero = sem("ident_zero")
        ident_ready = sem("ident_ready")
        toep_hi_ready = sem("toep_hi_ready")
        toep_lo_ready = sem("toep_lo_ready")
        cond_t_ps = sem("cond_t_ps")
        cond_t_ready = sem("cond_t_ready")
        ctx_ps = sem("ctx_ps")
        row_bias_ready = sem("row_bias_ready")
        b_col_ready = sem("b_col_ready")
        bt_ps = sem("bt_ps")
        bt_ready = sem("bt_ready")
        wt_ps = sem("wt_ps")
        wt_hi_ready = sem("wt_hi_ready")
        wt_lo_ready = sem("wt_lo_ready")
        xres_ready = sem("xres_ready")
        xtile_ready = sem("xtile_ready")
        xt_ps = sem("xt_ps")
        xt_hi_ready = sem("xt_hi_ready")
        xt_lo_ready = sem("xt_lo_ready")
        conv_ps = sem("conv_ps")
        conv_ready = sem("conv_ready")
        ct_ps = sem("ct_ps")
        ct_hi_ready = sem("ct_hi_ready")
        ct_lo_ready = sem("ct_lo_ready")
        y_ps = sem("y_ps")
        y_ready = sem("y_ready")
        out_done = sem("out_done")

        def nth(g, i):
            return CG * g + i

        def wait_for(eng, s, count):
            if not isinstance(count, int) or count > 0:
                eng.wait_ge(s, count)

        def toep_fwd(g):
            return toep_rev[:, g, :, ::-1].rearrange("p o j -> p j o")

        def by_tiles(g, q):
            part = xres[:, bass.ds(nth(g, 0), CG), q * CHUNK:(q + 1) * CHUNK]
            return part.rearrange("p c (t s) -> p t c s", s=S)

        def tile_slot(q):
            return xtile[:, q % RING, :, :].rearrange("p t (c s) -> p t c s", s=S)

        block = ctx.enter_context(nc.Block())

        @block.sync
        def _(sp):
            quarter = L // 4
            for i in range(4):
                sp.dma_start(xres[:, 0:CG, i * quarter:(i + 1) * quarter],
                             x[:, 0:CG, i * quarter:(i + 1) * quarter]).then_inc(x0_in[i], 16)
            sp.dma_start(w_nat[:], ffn_w.rearrange("(p t) l -> p t l", t=MT)).then_inc(w_in, 16)
            sp.dma_start(a_nat[:], lora_a.rearrange("i r l -> (i r) l")).then_inc(a_in, 16)
            sp.dma_start(ffn_bias_rows[:], ffn_bias.rearrange("(a m) -> a m", a=1).to_broadcast([P, M])
                         ).then_inc(ffn_bias_in, 16)
            for g in range(1, GROUPS):
                if g > 1:
                    sp.wait_ge(x_in, 16 * (g - 1))
                sp.dma_start(xres[:, g * CG:(g + 1) * CG, :], x[:, g * CG:(g + 1) * CG, :]).then_inc(x_in, 16)

            def store_pair(g, o):
                sp.wait_ge(y_ready, nth(g, o + 2))
                sp.dma_start(out[:, bass.ds(nth(g, o), 2), :],
                             xres[:, bass.ds(nth(g, o), 2), :]).then_inc(out_done, 16)

            with sp.Fori(0, GROUPS) as g:
                for o in range(0, CG, 2):
                    store_pair(g, o)
            sp.wait_ge(out_done, 16 * C // 2)

        @block.gpsimd
        def _(pool):
            nc.gpsimd.memset(toep_rev[:], 0.0).then_inc(toep_zero, 1)
            nc.gpsimd.memset(ident[:], 0.0).then_inc(ident_zero, 1)
            pool.wait_ge(ident_zero, 1)
            nc.gpsimd.affine_select(out=ident[:], in_=ident[:], compare_op=ALU.not_equal, fill=1.0, base=0,
                                    pattern=[[-1, P]], channel_multiplier=1).then_inc(ident_ready, 1)
            pool.wait_ge(b_in, 16)
            nc.gpsimd.tensor_copy(b_col[:].rearrange("p t (i r) -> p i t r", i=NL), b_nat[:]
                                  ).then_inc(b_col_ready, 1)
            pool.wait_ge(ffn_bias_in, 16)

            PIECE = CG // 4

            def add_bias(g, i):
                part = xres[:, bass.ds(nth(g, PIECE * i), PIECE), :]
                nc.gpsimd.tensor_tensor(part, part, ffn_bias_rows[:].unsqueeze(1).to_broadcast([P, PIECE, M]),
                                        ALU.add).then_inc(xres_ready, 1)

            pool.wait_ge(xtile_ready, Q)
            for i in range(4):
                add_bias(0, i)
            with pool.Fori(1, GROUPS) as g:
                pool.wait_ge(x_in, 16 * g)
                for q in range(Q):
                    pool.wait_ge(xt_ps, nth(g, q - RING + 1))
                    nc.gpsimd.tensor_copy(tile_slot(q), by_tiles(g, q)).then_inc(xtile_ready, 1)
                pool.wait_ge(xtile_ready, nth(g, Q))
                for i in reversed(range(4)):
                    add_bias(g, i)

        @block.scalar
        def _(act):
            act.dma_start(cond_nat[:], cond).then_inc(cond_in, 16)
            act.dma_start(ctxw_nat[:], ctx_w).then_inc(cond_in, 16)
            act.dma_start(chan_bias_rows[:], chan_bias.rearrange("(a m) -> a m", a=1).to_broadcast([P, C])
                          ).then_inc(chan_bias_in, 16)
            act.wait_ge(toep_zero, 1)
            for s in range(S):
                act.dma_start(toep_rev[s:s + S * (CG - 1) + 1:S, :, :, S - 1 - s:S - 1 - s + TAPS]
                              .rearrange("c g o k -> c (g o) k"),
                              conv_w.rearrange("o c k -> c o k")).then_inc(toep_in, 16)
            act.dma_start(b_nat[:], lora_b.rearrange("i (p t) r -> p i t r", t=MT)).then_inc(b_in, 16)
            for i in range(NL):
                act.dma_start(lw_col[i * RANK:(i + 1) * RANK, :],
                              lora_weights[i:i + 1].rearrange("(i a) -> i a", a=1).to_broadcast([RANK, 1])
                              ).then_inc(lw_in, 16)

            def x_hi(g, q):
                n = nth(g, q)
                act.wait_ge(xt_ps, n + 1)
                wait_for(act, conv_ps, n - RING + 2)
                nc.scalar.copy(xt_hi[:, q % RING, :], ps_xt[:, q % 2, :]).then_inc(xt_hi_ready, 1)

            def c_hi(g, o):
                act.wait_ge(ct_ps, nth(g, o + 1))
                nc.scalar.copy(ct_hi[:, o, :], ps_ct[:, o % 2, :]).then_inc(ct_hi_ready, 1)

            def order_x(q):
                act.wait_ge(x0_in[q // 2], 16)
                wait_for(act, xt_ps, q - RING + 1)
                nc.scalar.copy(tile_slot(q), by_tiles(0, q)).then_inc(xtile_ready, 1)

            order_x(0)
            order_x(1)
            x_hi(0, 0)
            order_x(2)
            x_hi(0, 1)
            order_x(3)
            act.wait_ge(toep_in, 16 * S)
            for g in range(GROUPS):
                nc.scalar.copy(toep_hi[:, g, :, :], toep_fwd(g)).then_inc(toep_hi_ready, 1)
            act.wait_ge(cond_t_ps, 2)
            nc.scalar.copy(cond_t[:], ps_ct[:, 0, 0:P + C]).then_inc(cond_t_ready, 1)
            for q in range(2, Q):
                x_hi(0, q)
                if q + 2 < Q:
                    order_x(q + 2)
            for lt in range(KT):
                act.wait_ge(wt_ps, lt + 1)
                nc.scalar.copy(wt_hi[:, lt, :], ps_y[:, lt % 2, :].rearrange("l (t p) -> l p t", t=MT)
                               ).then_inc(wt_hi_ready, 1)
            for o in range(CG // 2):
                c_hi(0, o)
            with act.Fori(1, GROUPS) as g:
                x_hi(g, 0)
                c_hi(g - 1, 4)
                x_hi(g, 1)
                c_hi(g - 1, 5)
                c_hi(g - 1, 6)
                x_hi(g, 2)
                c_hi(g - 1, 7)
                for q in range(3, Q):
                    x_hi(g, q)
                for o in range(CG // 2):
                    c_hi(g, o)
            for o in range(CG // 2, CG):
                c_hi(GROUPS - 1, o)

        @block.vector
        def _(dve):
            def x_lo(g, q):
                dve.wait_ge(xt_hi_ready, nth(g, q + 1))
                nc.vector.tensor_tensor(xt_lo[:, q % RING, :], ps_xt[:, q % 2, :],
                                        xt_hi[:, q % RING, :].bitcast(F32), ALU.subtract).then_inc(xt_lo_ready, 1)

            def c_lo(g, o):
                dve.wait_ge(ct_hi_ready, nth(g, o + 1))
                nc.vector.tensor_tensor(ct_lo[:, o, :], ps_ct[:, o % 2, :],
                                        ct_hi[:, o, :].bitcast(F32), ALU.subtract).then_inc(ct_lo_ready, 1)

            def conv_out(g, q):
                dve.wait_ge(conv_ps, nth(g, q + 1))
                if q == 0:
                    wait_for(dve, ct_ps, nth(g, 0))
                nc.vector.tensor_tensor(
                    conv[:, :, q * CHUNK:(q + 1) * CHUNK],
                    ps_conv[:, q % 2, :].rearrange("p (l o) -> p o l", o=CG),
                    row_bias[:, bass.ds(g * CG, CG)].unsqueeze(2).to_broadcast([P, CG, CHUNK]),
                    ALU.add).then_inc(conv_ready, 1)

            def y_out(g, o):
                dve.wait_ge(y_ps, nth(g, o + 1))
                if o == 0:
                    dve.wait_ge(xres_ready, 4 * g + 4)
                row = xres[:, bass.ds(nth(g, o), 1), :].rearrange("p a m -> p (a m)")
                nc.vector.tensor_tensor(row, ps_y[:, o % 2, :], row, ALU.add).then_inc(y_ready, 1)

            x_lo(0, 0)
            x_lo(0, 1)
            for g in range(GROUPS):
                dve.wait_ge(toep_hi_ready, g + 1)
                nc.vector.tensor_tensor(toep_lo[:, g, :, :], toep_fwd(g), toep_hi[:, g, :, :].bitcast(F32),
                                        ALU.subtract).then_inc(toep_lo_ready, 1)
            dve.wait_ge(ctx_ps, 1)
            dve.wait_ge(chan_bias_in, 16)
            nc.vector.tensor_tensor(row_bias[:], ps_ct[:, 1, 0:C], chan_bias_rows[:], ALU.add
                                    ).then_inc(row_bias_ready, 1)
            dve.wait_ge(row_bias_ready, 1)
            x_lo(0, 2)
            for q in range(3, Q):
                conv_out(0, q - 3)
                x_lo(0, q)
            for q in range(Q - 3, Q):
                conv_out(0, q)
            dve.wait_ge(bt_ps, 1)
            dve.wait_ge(lw_in, 16 * NL)
            nc.vector.tensor_scalar(bt[:], ps_ct[:, 0, :], lw_col[:, 0:1], LORA_SCALE, ALU.mult, ALU.mult
                                    ).then_inc(bt_ready, 1)
            for lt in range(KT):
                dve.wait_ge(wt_hi_ready, lt + 1)
                nc.vector.tensor_tensor(wt_lo[:, lt, :], ps_y[:, lt % 2, :].rearrange("l (t p) -> l p t", t=MT),
                                        wt_hi[:, lt, :].bitcast(F32), ALU.subtract).then_inc(wt_lo_ready, 1)
            for o in range(CG // 2):
                c_lo(0, o)
            with dve.Fori(1, GROUPS) as g:
                x_lo(g, 0)
                y_out(g - 1, 0)
                c_lo(g - 1, 4)
                x_lo(g, 1)
                y_out(g - 1, 1)
                c_lo(g - 1, 5)
                c_lo(g - 1, 6)
                x_lo(g, 2)
                y_out(g - 1, 2)
                c_lo(g - 1, 7)
                conv_out(g, 0)
                x_lo(g, 3)
                conv_out(g, 1)
                x_lo(g, 4)
                y_out(g - 1, 3)
                conv_out(g, 2)
                x_lo(g, 5)
                conv_out(g, 3)
                x_lo(g, 6)
                y_out(g - 1, 4)
                conv_out(g, 4)
                x_lo(g, 7)
                conv_out(g, 5)
                y_out(g - 1, 5)
                conv_out(g, 6)
                conv_out(g, 7)
                y_out(g - 1, 6)
                c_lo(g, 0)
                c_lo(g, 1)
                y_out(g - 1, 7)
                c_lo(g, 2)
                c_lo(g, 3)
            last = GROUPS - 1
            y_out(last, 0)
            c_lo(last, 4)
            y_out(last, 1)
            c_lo(last, 5)
            c_lo(last, 6)
            y_out(last, 2)
            c_lo(last, 7)
            for o in range(3, CG):
                y_out(last, o)

        @block.tensor
        def _(pe):
            def transpose_x(g, q):
                n = nth(g, q)
                pe.wait_ge(xtile_ready, n + 1)
                wait_for(pe, xt_lo_ready, n - 1)
                for t in range(TPC):
                    mm = nc.tensor.transpose(ps_xt[:, q % 2, t * P:(t + 1) * P], xtile[:, q % RING, t, :], ident[:])
                mm.then_inc(xt_ps, 1)

            def convolve(g, q):
                n = nth(g, q)
                pe.wait_ge(xt_lo_ready, nth(g, min(q + 2, Q)))
                wait_for(pe, conv_ready, n - 1)
                first = True
                for t in range(max(q * TPC - 1, 0), min((q + 1) * TPC + 1, TILES)):
                    reach = t * S - PAD - q * CHUNK
                    lo, hi = max(reach, 0), min(reach + J, CHUNK)
                    slot, col = t // TPC % RING, t % TPC * P
                    for xt, toep in ((xt_hi, toep_hi), (xt_hi, toep_lo), (xt_lo, toep_hi)):
                        mm = nc.tensor.matmul(
                            ps_conv[:, q % 2, lo * CG:hi * CG],
                            xt[:, slot, col:col + P],
                            toep[:, bass.ds(g, 1), lo - reach:hi - reach, :].rearrange("p a j o -> p (a j o)"),
                            start=first, stop=False, skip_group_check=True)
                        first = False
                mm.then_inc(conv_ps, 1)

            def transpose_conv(g, o):
                n = nth(g, o)
                if o == 0:
                    pe.wait_ge(conv_ready, nth(g, Q))
                wait_for(pe, ct_lo_ready, n - 1)
                for lt in range(KT):
                    mm = nc.tensor.transpose(ps_ct[:, o % 2, lt * P:(lt + 1) * P],
                                             conv[:, o, lt * P:(lt + 1) * P], ident[:])
                mm.then_inc(ct_ps, 1)

            def ffn(g, o):
                n = nth(g, o)
                if o < 2:
                    pe.wait_ge(ct_lo_ready, nth(g, CG // 2))
                else:
                    pe.wait_ge(ct_lo_ready, n + 1)
                    pe.wait_ge(y_ready, n - 1)
                for lt in range(KT):
                    for ct, wt in ((ct_hi, wt_hi), (ct_hi, wt_lo), (ct_lo, wt_hi)):
                        mm = nc.tensor.matmul(ps_y[:, o % 2, :], ct[:, o, lt * P:(lt + 1) * P], wt[:, lt, :],
                                              start=(lt == 0 and ct is ct_hi and wt is wt_hi),
                                              stop=(lt == KT - 1 and ct is ct_lo))
                mm.then_inc(y_ps, 1)

            pe.wait_ge(ident_ready, 1)
            transpose_x(0, 0)
            transpose_x(0, 1)
            pe.wait_ge(cond_in, 32)
            nc.tensor.transpose(ps_ct[:, 0, 0:P], cond_nat[:], ident[:]).then_inc(cond_t_ps, 1)
            nc.tensor.transpose(ps_ct[:, 0, P:P + C], ctxw_nat[:], ident[0:C, 0:C]).then_inc(cond_t_ps, 1)
            pe.wait_ge(cond_t_ready, 1)
            nc.tensor.matmul(ps_ct[:, 1, 0:C], cond_t[:, 0:P], cond_t[:, P:P + C], start=True, stop=True
                             ).then_inc(ctx_ps, 1)
            transpose_x(0, 2)
            pe.wait_ge(toep_lo_ready, GROUPS)
            for q in range(3, Q):
                convolve(0, q - 3)
                transpose_x(0, q)
            for q in range(Q - 3, Q):
                convolve(0, q)
            pe.wait_ge(b_col_ready, 1)
            for t in range(MT):
                mm = nc.tensor.transpose(ps_ct[:, 0, t * P:(t + 1) * P], b_col[:, t, :], ident[:])
            mm.then_inc(bt_ps, 1)
            pe.wait_ge(w_in, 16)
            pe.wait_ge(a_in, 16)
            pe.wait_ge(bt_ready, 1)
            for lt in range(KT):
                wait_for(pe, wt_lo_ready, lt - 1)
                for t in range(MT):
                    nc.tensor.matmul(ps_y[:, lt % 2, t * P:(t + 1) * P], w_nat[:, t, lt * P:(lt + 1) * P], ident[:],
                                     start=(t == 0), stop=False, skip_group_check=True)
                nc.tensor.matmul(ps_y[:, lt % 2, :], a_nat[:, lt * P:(lt + 1) * P], bt[:],
                                 start=False, stop=True, skip_group_check=True).then_inc(wt_ps, 1)
            for o in range(CG // 2):
                transpose_conv(0, o)
            pe.wait_ge(wt_lo_ready, KT)
            with pe.Fori(1, GROUPS) as g:
                transpose_x(g, 0)
                ffn(g - 1, 0)
                transpose_conv(g - 1, 4)
                transpose_x(g, 1)
                ffn(g - 1, 1)
                transpose_conv(g - 1, 5)
                transpose_conv(g - 1, 6)
                transpose_x(g, 2)
                ffn(g - 1, 2)
                transpose_conv(g - 1, 7)
                convolve(g, 0)
                transpose_x(g, 3)
                transpose_x(g, 4)
                convolve(g, 1)
                ffn(g - 1, 3)
                convolve(g, 2)
                transpose_x(g, 5)
                transpose_x(g, 6)
                convolve(g, 3)
                ffn(g - 1, 4)
                convolve(g, 4)
                transpose_x(g, 7)
                convolve(g, 5)
                ffn(g - 1, 5)
                convolve(g, 6)
                convolve(g, 7)
                ffn(g - 1, 6)
                transpose_conv(g, 0)
                transpose_conv(g, 1)
                ffn(g - 1, 7)
                transpose_conv(g, 2)
                transpose_conv(g, 3)
            last = GROUPS - 1
            ffn(last, 0)
            transpose_conv(last, 4)
            ffn(last, 1)
            transpose_conv(last, 5)
            transpose_conv(last, 6)
            ffn(last, 2)
            transpose_conv(last, 7)
            for o in range(3, CG):
                ffn(last, o)


_INS = ['x', 'cond_128', 'fside_S_0', 'L0_cond_weight', 'L0_cond_c_weight', 'L0_ffn_lora_A', 'L0_ffn_lora_B',
        'L0_ffn_W', 'L0_ffn_bias', 'L0_ffn_lora_weights']
_OUTS = [((128, 32, 512), 'float32')]


def kernel(**inputs):
    import numpy as _np
    import concourse.bacc as _bacc
    from concourse import mybir as _mybir
    from concourse.bass_utils import run_bass_kernel_spmd as _run

    nc = _bacc.Bacc("TRN2", target_bir_lowering=False, num_devices=1)
    arrays, args = {}, []
    for name in _INS:
        a = _np.ascontiguousarray(inputs[name])
        arrays[f"in_{name}_dram"] = a
        args.append(nc.dram_tensor(f"in_{name}_dram", a.shape, _mybir.dt.from_np(a.dtype), kind="ExternalInput").ap())
    for i, (shape, dtype) in enumerate(_OUTS):
        dt = _mybir.dt.from_np(_np.dtype(dtype))
        args.append(nc.dram_tensor(f"out_{i}_dram", shape, dt, kind="ExternalOutput").ap())
    adaln_ffn(nc, *args)
    r = _run(nc, [arrays], core_ids=[0])
    got = tuple(r.results[0][f"out_{i}_dram"] for i in range(len(_OUTS)))
    return got[0]
```

```python
from contextlib import ExitStack

import concourse.bass as bass
from concourse import mybir

ALU = mybir.AluOpType
ACT = mybir.ActivationFunctionType
F32 = mybir.dt.float32
F32R = mybir.dt.float32r

P = 128


def adaln_ffn(
    nc: bass.Bass,
    x: bass.AP,
    cond: bass.AP,
    chan_bias: bass.AP,
    conv_w: bass.AP,
    ctx_w: bass.AP,
    lora_a: bass.AP,
    lora_b: bass.AP,
    ffn_w: bass.AP,
    ffn_bias: bass.AP,
    lora_weights: bass.AP,
    out: bass.AP,
):
    N, C, L = x.shape
    OUT_CH, CG, TAPS = conv_w.shape
    GROUPS = C // CG
    NL, RANK, _ = lora_a.shape
    M = ffn_w.shape[0]
    LORA_SCALE = 32.0 / RANK
    S = P // CG
    PAD = TAPS // 2
    J = S + TAPS - 1
    CHUNK = 512 // CG
    Q = L // CHUNK
    TPC = CHUNK // S
    EDGE = PAD * CG
    KT = L // P
    MT = M // P
    RING = 4
    WARM_UP = 10
    TOEP_SP = 10
    assert N == P and OUT_CH == C and NL * RANK == P and Q == CG and Q % RING == 0 and M == 512

    with ExitStack() as ctx:
        def sb(name, shape, dt=F32):
            return ctx.enter_context(nc.sbuf_tensor(name, shape, dt))

        def ps(name, shape):
            return ctx.enter_context(nc.psum_tensor(name, shape, F32))

        def sem(name):
            return ctx.enter_context(nc.semaphore(name))

        ident = sb("ident", [P, P])
        xres = sb("xres", [P, C, L])
        xtile = sb("xtile", [P, RING, TPC, S * CG])
        xt = sb("xt", [P, Q, TPC * P])
        conv = sb("conv", [P, CG, L])
        ct_hi = sb("ct_hi", [P, CG, KT * P], F32R)
        ct_lo = sb("ct_lo", [P, CG, KT * P], F32R)
        wt_hi = sb("wt_hi", [P, KT, M], F32R)
        wt_lo = sb("wt_lo", [P, KT, M], F32R)
        toep_rev = sb("toep_rev", [P, GROUPS, CG, J])
        toep = sb("toep", [P, GROUPS, J, CG])
        toep_first = sb("toep_first", [P, GROUPS, J - 2 * PAD, CG])
        toep_wrap = sb("toep_wrap", [P, GROUPS, 2 * PAD, CG])
        w_nat = sb("w_nat", [P, MT, L])
        a_nat = sb("a_nat", [P, L])
        b_nat = sb("b_nat", [P, NL, MT, RANK])
        b_col = sb("b_col", [P, MT, NL * RANK])
        bt = sb("bt", [P, M])
        lw_rows = sb("lw_rows", [P, NL])
        cond_nat = sb("cond_nat", [P, P])
        ctxw_nat = sb("ctxw_nat", [C, P])
        cond_t = sb("cond_t", [P, P + C])
        chan_bias_rows = sb("chan_bias_rows", [P, C])
        row_bias = sb("row_bias", [P, C])
        ffn_bias_rows = sb("ffn_bias_rows", [P, M])

        ps_xt = ps("ps_xt", [P, 2, 512])
        ps_conv = ps("ps_conv", [P, 2, 512])
        ps_ct = ps("ps_ct", [P, 2, 512])
        ps_y = ps("ps_y", [P, 2, 512])

        x0_in = [sem(f"x0_in{i}") for i in range(4)]
        x_in = sem("x_in")
        toep_zero = sem("toep_zero")
        toep_in = sem("toep_in")
        toep_in_pool = sem("toep_in_pool")
        w_in = sem("w_in")
        a_in = sem("a_in")
        b_in = sem("b_in")
        lw_in = sem("lw_in")
        cond_in = sem("cond_in")
        chan_bias_in = sem("chan_bias_in")
        ffn_bias_in = sem("ffn_bias_in")
        ident_zero = sem("ident_zero")
        ident_ready = sem("ident_ready")
        toep_copied = sem("toep_copied")
        toep_ready = sem("toep_ready")
        cond_t_ps = sem("cond_t_ps")
        cond_t_ready = sem("cond_t_ready")
        ctx_ps = sem("ctx_ps")
        row_bias_ready = sem("row_bias_ready")
        b_col_ready = sem("b_col_ready")
        bt_ps = sem("bt_ps")
        bt_ready = sem("bt_ready")
        wt_ps = [sem(f"wt_ps{lt}") for lt in range(KT)]
        wt_hi_ready = [sem(f"wt_hi_ready{lt}") for lt in range(KT)]
        wt_lo_ready = [sem(f"wt_lo_ready{lt}") for lt in range(KT)]
        xres_ready = sem("xres_ready")
        xtile_ready = sem("xtile_ready")
        xt_ps = sem("xt_ps")
        xt_ready = sem("xt_ready")
        conv_ps = sem("conv_ps")
        conv_ready = sem("conv_ready")
        ct_ps = sem("ct_ps")
        ct_hi_ready = sem("ct_hi_ready")
        ct_lo_ready = sem("ct_lo_ready")
        y_ps = sem("y_ps")
        y_ready = sem("y_ready")
        out_done = sem("out_done")

        def nth(g, i):
            return CG * g + i

        def wait_for(eng, s, count):
            if not isinstance(count, int) or count > 0:
                eng.wait_ge(s, count)

        def load_toeplitz(eng, s, arrived):
            eng.dma_start(toep_rev[s * CG:(s + 1) * CG, :, :, S - 1 - s:S - 1 - s + TAPS]
                          .rearrange("c g o k -> c (g o) k"),
                          conv_w.rearrange("o c k -> c o k")).then_inc(arrived, 16)

        def x_part(g, lo, hi):
            part = xres[:, bass.ds(nth(g, 0), CG), lo:hi]
            return part.rearrange("p c (t s) -> p t c s", s=min(S, hi - lo))

        def tile_part(q, t0, t1, s0, s1):
            return xtile[:, q % RING, t0:t1, :].rearrange("p t (s c) -> p t c s", c=CG)[:, :, :, s0:s1]

        def w_bank(lt):
            return ps_y[:, lt, :] if lt < 2 else ps_conv[:, lt - 2, :]

        def order_x(eng, copy, g, q):
            wait_for(eng, xt_ps, nth(g, q - RING + 1))
            if q == 0:
                copy(tile_part(0, 0, 1, 0, PAD), x_part(g, L - PAD, L))
                copy(tile_part(0, 0, 1, PAD, S), x_part(g, 0, S - PAD))
                last = copy(tile_part(0, 1, TPC, 0, S), x_part(g, S - PAD, CHUNK - PAD))
            else:
                last = copy(tile_part(q, 0, TPC, 0, S), x_part(g, q * CHUNK - PAD, (q + 1) * CHUNK - PAD))
            last.then_inc(xtile_ready, 1)

        block = ctx.enter_context(nc.Block())

        @block.sync
        def _(sp):
            def load_quarter(i):
                part = slice(i * L // 4, (i + 1) * L // 4)
                sp.dma_start(xres[:, 0:CG, part], x[:, 0:CG, part]).then_inc(x0_in[i], 16)

            sp.dma_start(w_nat[:], ffn_w.rearrange("(p t) l -> p t l", t=MT)).then_inc(w_in, 16)
            sp.dma_start(a_nat[:], lora_a.rearrange("i r l -> (i r) l")).then_inc(a_in, 16)
            load_quarter(0)
            load_quarter(3)
            sp.wait_ge(toep_zero, 1)
            for s in range(TOEP_SP):
                load_toeplitz(sp, s, toep_in)
            load_quarter(1)
            sp.dma_start(cond_nat[:], cond).then_inc(cond_in, 16)
            sp.dma_start(ctxw_nat[:], ctx_w).then_inc(cond_in, 16)
            sp.dma_start(chan_bias_rows[:], chan_bias.rearrange("(a m) -> a m", a=1).to_broadcast([P, C])
                         ).then_inc(chan_bias_in, 16)
            load_quarter(2)
            sp.dma_start(ffn_bias_rows[:], ffn_bias.rearrange("(a m) -> a m", a=1).to_broadcast([P, M])
                         ).then_inc(ffn_bias_in, 16)
            for g in range(1, GROUPS):
                if g > 1:
                    sp.wait_ge(x_in, 16 * (g - 1))
                sp.dma_start(xres[:, g * CG:(g + 1) * CG, :], x[:, g * CG:(g + 1) * CG, :]).then_inc(x_in, 16)

            def store(g, o, channels):
                sp.wait_ge(y_ready, nth(g, o + channels))
                sp.dma_start(out[:, bass.ds(nth(g, o), channels), :],
                             xres[:, bass.ds(nth(g, o), channels), :]).then_inc(out_done, 16)

            with sp.Fori(0, GROUPS - 1) as g:
                for o in range(0, CG, 2):
                    store(g, o, 2)
            for o in range(0, CG - 2, 2):
                store(GROUPS - 1, o, 2)
            store(GROUPS - 1, CG - 2, 1)
            store(GROUPS - 1, CG - 1, 1)
            sp.wait_ge(out_done, 16 * (C // 2 + 1))

        @block.gpsimd
        def _(pool):
            nc.gpsimd.memset(toep_rev[:], 0.0).then_inc(toep_zero, 1)
            nc.gpsimd.memset(ident[:], 0.0).then_inc(ident_zero, 1)
            pool.wait_ge(ident_zero, 1)
            nc.gpsimd.affine_select(out=ident[:], in_=ident[:], compare_op=ALU.not_equal, fill=1.0, base=0,
                                    pattern=[[-1, P]], channel_multiplier=1).then_inc(ident_ready, 1)
            for s in range(TOEP_SP, S):
                load_toeplitz(pool, s, toep_in_pool)
            pool.wait_ge(ffn_bias_in, 16)

            PIECE = CG // 4

            def add_bias(g, i):
                part = xres[:, bass.ds(nth(g, PIECE * i), PIECE), :]
                nc.gpsimd.tensor_tensor(part, part, ffn_bias_rows[:].unsqueeze(1).to_broadcast([P, PIECE, M]),
                                        ALU.add).then_inc(xres_ready, 1)

            pool.wait_ge(xtile_ready, Q)
            for i in range(4):
                add_bias(0, i)
            with pool.Fori(1, GROUPS) as g:
                pool.wait_ge(xtile_ready, nth(g, Q))
                for i in reversed(range(4)):
                    add_bias(g, i)

        @block.scalar
        def _(act):
            act.dma_start(b_nat[:], lora_b.rearrange("i (p t) r -> p i t r", t=MT)).then_inc(b_in, 16)
            act.dma_start(lw_rows[:], lora_weights.rearrange("(a i) -> a i", a=1).to_broadcast([P, NL])
                          ).then_inc(lw_in, 16)
            def xt_out(g, q):
                act.wait_ge(xt_ps, nth(g, q + 1))
                nc.scalar.copy(xt[:, q, :], ps_xt[:, q % 2, :]).then_inc(xt_ready, 1)

            def c_hi(g, o):
                act.wait_ge(ct_ps, nth(g, o + 1))
                nc.scalar.copy(ct_hi[:, o, :], ps_ct[:, o % 2, :]).then_inc(ct_hi_ready, 1)

            def w_hi(lt):
                act.wait_ge(wt_ps[lt], 1)
                nc.scalar.copy(wt_hi[:, lt, :], w_bank(lt).rearrange("l (t p) -> l p t", t=MT)
                               ).then_inc(wt_hi_ready[lt], 1)

            act.wait_ge(x0_in[0], 16)
            act.wait_ge(x0_in[3], 16)
            order_x(act, nc.scalar.copy, 0, 0)
            order_x(act, nc.scalar.copy, 0, 1)
            w_hi(2)
            xt_out(0, 0)
            w_hi(3)
            xt_out(0, 1)
            act.wait_ge(cond_t_ps, 2)
            nc.scalar.copy(cond_t[:], ps_ct[:, 0, 0:P + C]).then_inc(cond_t_ready, 1)
            act.wait_ge(x0_in[1], 16)
            order_x(act, nc.scalar.copy, 0, 2)
            order_x(act, nc.scalar.copy, 0, 3)
            xt_out(0, 2)
            act.wait_ge(x0_in[2], 16)
            order_x(act, nc.scalar.copy, 0, 4)
            xt_out(0, 3)
            for q in range(4, Q):
                if q + 1 < Q:
                    order_x(act, nc.scalar.copy, 0, q + 1)
                xt_out(0, q)
            w_hi(0)
            w_hi(1)
            for o in range(2):
                c_hi(0, o)
            with act.Fori(1, GROUPS) as g:
                act.wait_ge(x_in, 16 * g)
                order_x(act, nc.scalar.copy, g, 0)
                c_hi(g - 1, 2)
                xt_out(g, 0)
                order_x(act, nc.scalar.copy, g, 1)
                c_hi(g - 1, 3)
                c_hi(g - 1, 4)
                c_hi(g - 1, 5)
                xt_out(g, 1)
                order_x(act, nc.scalar.copy, g, 2)
                c_hi(g - 1, 6)
                c_hi(g - 1, 7)
                for q in range(2, Q - 1):
                    order_x(act, nc.scalar.copy, g, q + 1)
                    xt_out(g, q)
                xt_out(g, Q - 1)
                c_hi(g, 0)
                c_hi(g, 1)
            for o in range(2, CG):
                c_hi(GROUPS - 1, o)

        @block.vector
        def _(dve):
            def c_lo(g, o):
                dve.wait_ge(ct_hi_ready, nth(g, o + 1))
                nc.vector.tensor_tensor(ct_lo[:, o, :], ps_ct[:, o % 2, :],
                                        ct_hi[:, o, :].bitcast(F32), ALU.subtract).then_inc(ct_lo_ready, 1)

            def conv_out(g, q):
                dve.wait_ge(conv_ps, nth(g, q + 1))
                if q == 0:
                    wait_for(dve, ct_ps, nth(g, 0))
                nc.vector.tensor_tensor(
                    conv[:, :, q * CHUNK:(q + 1) * CHUNK],
                    ps_conv[:, q % 2, :].rearrange("p (l o) -> p o l", o=CG),
                    row_bias[:, bass.ds(g * CG, CG)].unsqueeze(2).to_broadcast([P, CG, CHUNK]),
                    ALU.add).then_inc(conv_ready, 1)

            def y_out(g, o):
                dve.wait_ge(y_ps, nth(g, o + 1))
                if o == 0:
                    dve.wait_ge(xres_ready, 4 * g + 4)
                row = xres[:, bass.ds(nth(g, o), 1), :].rearrange("p a m -> p (a m)")
                nc.vector.tensor_tensor(row, ps_y[:, o % 2, :], row, ALU.add).then_inc(y_ready, 1)

            def w_lo(lt):
                dve.wait_ge(wt_hi_ready[lt], 1)
                nc.vector.tensor_tensor(wt_lo[:, lt, :], w_bank(lt).rearrange("l (t p) -> l p t", t=MT),
                                        wt_hi[:, lt, :].bitcast(F32), ALU.subtract).then_inc(wt_lo_ready[lt], 1)

            nc.vector.memset(toep_wrap[:], 0.0).then_inc(toep_copied, 1)
            dve.wait_ge(b_in, 16)
            dve.wait_ge(lw_in, 16)
            for t in range(MT):
                nc.vector.tensor_tensor(b_col[:, t, :].rearrange("p (i r) -> p i r", i=NL), b_nat[:, :, t, :],
                                        lw_rows[:].unsqueeze(2).to_broadcast([P, NL, RANK]), ALU.mult
                                        ).then_inc(b_col_ready, 1)
            dve.wait_ge(bt_ps, 1)
            nc.vector.tensor_scalar(bt[:], ps_ct[:, 1, :], LORA_SCALE, None, ALU.mult).then_inc(bt_ready, 1)
            dve.wait_ge(toep_in, 16 * TOEP_SP)
            dve.wait_ge(toep_in_pool, 16 * (S - TOEP_SP))
            for g in range(GROUPS):
                nc.vector.tensor_copy(toep[:, g, :, :], toep_rev[:, g, :, ::-1].rearrange("p o j -> p j o")
                                      ).then_inc(toep_copied, 1)
            dve.wait_ge(toep_copied, GROUPS + 1)
            nc.vector.tensor_copy(toep_first[:], toep[:, :, 2 * PAD:J, :]).then_inc(toep_copied, 1)
            nc.vector.tensor_copy(toep_wrap[0:EDGE], toep[0:EDGE, :, 0:2 * PAD, :]).then_inc(toep_ready, 1)
            dve.wait_ge(toep_copied, GROUPS + 2)
            nc.vector.memset(toep_first[0:EDGE], 0.0).then_inc(toep_ready, 1)
            w_lo(2)
            w_lo(3)
            dve.wait_ge(ctx_ps, 1)
            dve.wait_ge(chan_bias_in, 16)
            nc.vector.tensor_tensor(row_bias[:], ps_ct[:, 1, 0:C], chan_bias_rows[:], ALU.add
                                    ).then_inc(row_bias_ready, 1)
            dve.wait_ge(row_bias_ready, 1)
            for q in range(Q - 1):
                conv_out(0, q)
            w_lo(0)
            conv_out(0, Q - 1)
            w_lo(1)
            for o in range(2):
                c_lo(0, o)
            with dve.Fori(1, GROUPS) as g:
                y_out(g - 1, 0)
                c_lo(g - 1, 2)
                c_lo(g - 1, 3)
                y_out(g - 1, 1)
                c_lo(g - 1, 4)
                c_lo(g - 1, 5)
                y_out(g - 1, 2)
                c_lo(g - 1, 6)
                c_lo(g - 1, 7)
                y_out(g - 1, 3)
                conv_out(g, 0)
                conv_out(g, 1)
                y_out(g - 1, 4)
                conv_out(g, 2)
                conv_out(g, 3)
                y_out(g - 1, 5)
                conv_out(g, 4)
                conv_out(g, 5)
                conv_out(g, 6)
                conv_out(g, 7)
                y_out(g - 1, 6)
                c_lo(g, 0)
                y_out(g - 1, 7)
                c_lo(g, 1)
            last = GROUPS - 1
            for o in range(CG):
                y_out(last, o)
                if o + 2 < CG:
                    c_lo(last, o + 2)

        @block.tensor
        def _(pe):
            def transpose_x(g, q):
                n = nth(g, q)
                pe.wait_ge(xtile_ready, n + 1)
                wait_for(pe, xt_ready, n - 1)
                for t in range(TPC):
                    mm = nc.tensor.transpose(ps_xt[:, q % 2, t * P:(t + 1) * P], xtile[:, q % RING, t, :], ident[:])
                mm.then_inc(xt_ps, 1)

            def convolve(g, q):
                n = nth(g, q)
                pe.wait_ge(xt_ready, nth(g, min(q + 2, Q)))
                wait_for(pe, conv_ready, n - 1)

                def product(slot, tile, matrix, lo, hi, start=False):
                    return nc.tensor.matmul(ps_conv[:, q % 2, lo * CG:hi * CG], xt[:, slot, tile * P:(tile + 1) * P],
                                            matrix.rearrange("p a j o -> p (a j o)"),
                                            start=start, stop=False, skip_group_check=True)

                here = bass.ds(g, 1)
                if q == 0:
                    product(q, 0, toep_first[:, here, :, :], 0, J - 2 * PAD, start=True)
                else:
                    product(q, 0, toep[:, here, 2 * PAD:J, :], 0, J - 2 * PAD, start=True)
                for t in range(1, TPC):
                    product(q, t, toep[:, here, :, :], t * S - 2 * PAD, t * S - 2 * PAD + J)
                if q < Q - 1:
                    mm = product(q + 1, 0, toep[:, here, 0:2 * PAD, :], CHUNK - 2 * PAD, CHUNK)
                else:
                    mm = product(0, 0, toep_wrap[:, here, :, :], CHUNK - 2 * PAD, CHUNK)
                mm.then_inc(conv_ps, 1)

            def transpose_conv(g, o):
                n = nth(g, o)
                wait_for(pe, ct_lo_ready, n - 1)
                for lt in range(KT):
                    if o == 0 and lt == 0:
                        pe.wait_ge(conv_ready, nth(g, Q - Q // KT))
                    if o == 0 and lt == KT - 1:
                        pe.wait_ge(conv_ready, nth(g, Q))
                    mm = nc.tensor.transpose(ps_ct[:, o % 2, lt * P:(lt + 1) * P],
                                             conv[:, o, lt * P:(lt + 1) * P], ident[:])
                mm.then_inc(ct_ps, 1)

            def ffn(g, o):
                n = nth(g, o)
                pe.wait_ge(ct_lo_ready, n + 1)
                if o > 1:
                    pe.wait_ge(y_ready, n - 1)
                for lt in range(KT):
                    for ct, wt in ((ct_hi, wt_hi), (ct_hi, wt_lo), (ct_lo, wt_hi)):
                        mm = nc.tensor.matmul(ps_y[:, o % 2, :], ct[:, o, lt * P:(lt + 1) * P], wt[:, lt, :],
                                              start=(lt == 0 and ct is ct_hi and wt is wt_hi),
                                              stop=(lt == KT - 1 and ct is ct_lo))
                mm.then_inc(y_ps, 1)

            pe.wait_ge(ident_ready, 1)
            for _ in range(WARM_UP):
                nc.tensor.matmul(ps_ct[:, 1, 0:P], ident[:], ident[:], start=True, stop=True)
            pe.wait_ge(w_in, 16)
            for lt in range(KT):
                for t in range(MT):
                    nc.tensor.matmul(w_bank(lt)[:, t * P:(t + 1) * P], w_nat[:, t, lt * P:(lt + 1) * P], ident[:],
                                     start=(t == 0), stop=False, skip_group_check=True)
            pe.wait_ge(b_col_ready, MT)
            for t in range(MT):
                mm = nc.tensor.transpose(ps_ct[:, 1, t * P:(t + 1) * P], b_col[:, t, :], ident[:])
            mm.then_inc(bt_ps, 1)

            def add_lora(lt):
                nc.tensor.matmul(w_bank(lt), a_nat[:, lt * P:(lt + 1) * P], bt[:],
                                 start=False, stop=True, skip_group_check=True).then_inc(wt_ps[lt], 1)

            pe.wait_ge(a_in, 16)
            pe.wait_ge(bt_ready, 1)
            add_lora(2)
            transpose_x(0, 0)
            add_lora(3)
            transpose_x(0, 1)
            pe.wait_ge(cond_in, 32)
            nc.tensor.transpose(ps_ct[:, 0, 0:P], cond_nat[:], ident[:]).then_inc(cond_t_ps, 1)
            nc.tensor.transpose(ps_ct[:, 0, P:P + C], ctxw_nat[:], ident[0:C, 0:C]).then_inc(cond_t_ps, 1)
            pe.wait_ge(toep_ready, 2)
            for lt in range(2, KT):
                pe.wait_ge(wt_lo_ready[lt], 1)
            convolve(0, 0)
            transpose_x(0, 2)
            pe.wait_ge(cond_t_ready, 1)
            nc.tensor.matmul(ps_ct[:, 1, 0:C], cond_t[:, 0:P], cond_t[:, P:P + C], start=True, stop=True
                             ).then_inc(ctx_ps, 1)
            transpose_x(0, 3)
            convolve(0, 1)
            for q in range(4, Q):
                transpose_x(0, q)
                convolve(0, q - 2)
            convolve(0, Q - 2)
            add_lora(0)
            convolve(0, Q - 1)
            add_lora(1)
            transpose_conv(0, 0)
            transpose_conv(0, 1)
            for lt in range(2):
                pe.wait_ge(wt_lo_ready[lt], 1)
            with pe.Fori(1, GROUPS) as g:
                ffn(g - 1, 0)
                transpose_conv(g - 1, 2)
                transpose_x(g, 0)
                transpose_conv(g - 1, 3)
                ffn(g - 1, 1)
                transpose_conv(g - 1, 4)
                transpose_conv(g - 1, 5)
                transpose_x(g, 1)
                ffn(g - 1, 2)
                transpose_conv(g - 1, 6)
                transpose_conv(g - 1, 7)
                ffn(g - 1, 3)
                transpose_x(g, 2)
                convolve(g, 0)
                transpose_x(g, 3)
                convolve(g, 1)
                ffn(g - 1, 4)
                transpose_x(g, 4)
                convolve(g, 2)
                transpose_x(g, 5)
                convolve(g, 3)
                ffn(g - 1, 5)
                transpose_x(g, 6)
                convolve(g, 4)
                transpose_x(g, 7)
                convolve(g, 5)
                convolve(g, 6)
                convolve(g, 7)
                ffn(g - 1, 6)
                transpose_conv(g, 0)
                ffn(g - 1, 7)
                transpose_conv(g, 1)
            last = GROUPS - 1
            for o in range(CG):
                ffn(last, o)
                if o + 2 < CG:
                    transpose_conv(last, o + 2)


_INS = ['x', 'cond_128', 'fside_S_0', 'L0_cond_weight', 'L0_cond_c_weight', 'L0_ffn_lora_A', 'L0_ffn_lora_B',
        'L0_ffn_W', 'L0_ffn_bias', 'L0_ffn_lora_weights']
_OUTS = [((128, 32, 512), 'float32')]


def kernel(**inputs):
    import numpy as _np
    import concourse.bacc as _bacc
    from concourse import mybir as _mybir
    from concourse.bass_utils import run_bass_kernel_spmd as _run

    nc = _bacc.Bacc("TRN2", target_bir_lowering=False, num_devices=1)
    arrays, args = {}, []
    for name in _INS:
        a = _np.ascontiguousarray(inputs[name])
        arrays[f"in_{name}_dram"] = a
        args.append(nc.dram_tensor(f"in_{name}_dram", a.shape, _mybir.dt.from_np(a.dtype), kind="ExternalInput").ap())
    for i, (shape, dtype) in enumerate(_OUTS):
        dt = _mybir.dt.from_np(_np.dtype(dtype))
        args.append(nc.dram_tensor(f"out_{i}_dram", shape, dt, kind="ExternalOutput").ap())
    adaln_ffn(nc, *args)
    r = _run(nc, [arrays], core_ids=[0])
    got = tuple(r.results[0][f"out_{i}_dram"] for i in range(len(_OUTS)))
    return got[0]
```

```python
from contextlib import ExitStack

import concourse.bass as bass
from concourse import mybir

ALU = mybir.AluOpType
ACT = mybir.ActivationFunctionType
F32 = mybir.dt.float32
F32R = mybir.dt.float32r

P = 128


def adaln_ffn(
    nc: bass.Bass,
    x: bass.AP,
    cond: bass.AP,
    chan_bias: bass.AP,
    conv_w: bass.AP,
    ctx_w: bass.AP,
    lora_a: bass.AP,
    lora_b: bass.AP,
    ffn_w: bass.AP,
    ffn_bias: bass.AP,
    lora_weights: bass.AP,
    out: bass.AP,
):
    N, C, L = x.shape
    OUT_CH, CG, TAPS = conv_w.shape
    GROUPS = C // CG
    NL, RANK, _ = lora_a.shape
    M = ffn_w.shape[0]
    LORA_SCALE = 32.0 / RANK
    S = P // CG
    PAD = TAPS // 2
    J = S + TAPS - 1
    CHUNK = 512 // CG
    Q = L // CHUNK
    TPC = CHUNK // S
    EDGE = PAD * CG
    KT = L // P
    MT = M // P
    RING = 4
    WARM_UP = 8
    TOEP_SP = 10
    assert N == P and OUT_CH == C and NL * RANK == P and Q == CG and Q % RING == 0 and M == 512

    with ExitStack() as ctx:
        def sb(name, shape, dt=F32):
            return ctx.enter_context(nc.sbuf_tensor(name, shape, dt))

        def ps(name, shape):
            return ctx.enter_context(nc.psum_tensor(name, shape, F32))

        def sem(name):
            return ctx.enter_context(nc.semaphore(name))

        ident = sb("ident", [P, P])
        xres = sb("xres", [P, C, L])
        xtile = sb("xtile", [P, RING, TPC, S * CG])
        xt = sb("xt", [P, Q, TPC * P])
        conv = sb("conv", [P, CG, L])
        ct_hi = sb("ct_hi", [P, CG, KT * P], F32R)
        ct_lo = sb("ct_lo", [P, CG, KT * P], F32R)
        wt_hi = sb("wt_hi", [P, KT, M], F32R)
        wt_lo = sb("wt_lo", [P, KT, M], F32R)
        toep_rev = sb("toep_rev", [P, GROUPS, CG, J])
        toep = sb("toep", [P, GROUPS, J, CG])
        toep_first = sb("toep_first", [P, GROUPS, J - 2 * PAD, CG])
        toep_wrap = sb("toep_wrap", [P, GROUPS, 2 * PAD, CG])
        w_nat = sb("w_nat", [P, MT, L])
        w_t = sb("w_t", [P, KT, M])
        a_nat = sb("a_nat", [P, L])
        b_nat = sb("b_nat", [P, NL, MT, RANK])
        b_col = sb("b_col", [P, MT, NL * RANK])
        bt = sb("bt", [P, M])
        lw_rows = sb("lw_rows", [P, NL])
        cond_nat = sb("cond_nat", [P, P])
        ctxw_nat = sb("ctxw_nat", [C, P])
        cond_t = sb("cond_t", [P, P + C])
        chan_bias_rows = sb("chan_bias_rows", [P, C])
        row_bias = sb("row_bias", [P, C])
        ffn_bias_rows = sb("ffn_bias_rows", [P, M])
        table_scrap = sb("table_scrap", [P, 1])

        ps_xt = ps("ps_xt", [P, 2, 512])
        ps_conv = ps("ps_conv", [P, 2, 512])
        ps_ct = ps("ps_ct", [P, 2, 512])
        ps_y = ps("ps_y", [P, 2, 512])

        x0_in = [sem(f"x0_in{i}") for i in range(4)]
        x0_edge_in = sem("x0_edge_in")
        x_in = sem("x_in")
        toep_zero = sem("toep_zero")
        toep_in = sem("toep_in")
        toep_in_pool = sem("toep_in_pool")
        w_in = [sem(f"w_in{i}") for i in range(2)]
        a_in = sem("a_in")
        b_in = sem("b_in")
        lw_in = sem("lw_in")
        cond_in = sem("cond_in")
        chan_bias_in = sem("chan_bias_in")
        ffn_bias_in = sem("ffn_bias_in")
        ident_zero = sem("ident_zero")
        ident_ready = sem("ident_ready")
        toep_copied = sem("toep_copied")
        toep_ready = sem("toep_ready")
        cond_t_ps = sem("cond_t_ps")
        cond_t_ready = sem("cond_t_ready")
        ctx_ps = sem("ctx_ps")
        row_bias_ready = sem("row_bias_ready")
        b_col_ready = sem("b_col_ready")
        bt_ps = sem("bt_ps")
        bt_ready = sem("bt_ready")
        w_ps = [sem(f"w_ps{lt}") for lt in range(KT)]
        w_t_ready = [sem(f"w_t_ready{lt}") for lt in range(KT)]
        lora_ps = [sem(f"lora_ps{lt}") for lt in range(KT)]
        weff_ready = [sem(f"weff_ready{lt}") for lt in range(KT)]
        wt_hi_ready = [sem(f"wt_hi_ready{lt}") for lt in range(KT)]
        wt_lo_ready = [sem(f"wt_lo_ready{lt}") for lt in range(KT)]
        xres_ready = sem("xres_ready")
        xtile_ready = sem("xtile_ready")
        xt_ps = sem("xt_ps")
        xt_ready = sem("xt_ready")
        conv_ps = sem("conv_ps")
        conv_ready = sem("conv_ready")
        ct_ps = sem("ct_ps")
        ct_hi_ready = sem("ct_hi_ready")
        ct_lo_ready = sem("ct_lo_ready")
        y_ps = sem("y_ps")
        y_ready = sem("y_ready")
        out_done = sem("out_done")

        def nth(g, i):
            return CG * g + i

        def wait_for(eng, s, count):
            if not isinstance(count, int) or count > 0:
                eng.wait_ge(s, count)

        def load_toeplitz(eng, s, arrived):
            eng.dma_start(toep_rev[s * CG:(s + 1) * CG, :, :, S - 1 - s:S - 1 - s + TAPS]
                          .rearrange("c g o k -> c (g o) k"),
                          conv_w.rearrange("o c k -> c o k")).then_inc(arrived, 16)

        def x_part(g, lo, hi):
            part = xres[:, bass.ds(nth(g, 0), CG), lo:hi]
            return part.rearrange("p c (t s) -> p t c s", s=min(S, hi - lo))

        def tile_part(q, t0, t1, s0, s1):
            return xtile[:, q % RING, t0:t1, :].rearrange("p t (s c) -> p t c s", c=CG)[:, :, :, s0:s1]

        def w_bank(lt):
            return (ps_y if lt < 2 else ps_xt)[:, lt % 2, :]

        def lora_bank(lt):
            return (ps_ct if lt < 2 else ps_y)[:, lt % 2, :]

        def m_order(bank):
            return bank.rearrange("l (t p) -> l p t", t=MT)

        def w_out(eng, copy, lt):
            eng.wait_ge(w_ps[lt], 1)
            copy(w_t[:, lt, :], m_order(w_bank(lt))).then_inc(w_t_ready[lt], 1)

        def order_x(eng, copy, g, q):
            wait_for(eng, xt_ps, nth(g, q - RING + 1))
            if q == 0:
                copy(tile_part(0, 0, 1, 0, PAD), x_part(g, L - PAD, L))
                copy(tile_part(0, 0, 1, PAD, S), x_part(g, 0, S - PAD))
                last = copy(tile_part(0, 1, TPC, 0, S), x_part(g, S - PAD, CHUNK - PAD))
            else:
                last = copy(tile_part(q, 0, TPC, 0, S), x_part(g, q * CHUNK - PAD, (q + 1) * CHUNK - PAD))
            last.then_inc(xtile_ready, 1)

        block = ctx.enter_context(nc.Block())

        @block.sync
        def _(sp):
            def load_first(lo, hi, arrived):
                sp.dma_start(xres[:, 0:CG, lo:hi], x[:, 0:CG, lo:hi]).then_inc(arrived, 16)

            QUARTER = L // 4

            def load_w(half):
                cols = slice(half * L // 2, (half + 1) * L // 2)
                sp.dma_start(w_nat[:, :, cols], ffn_w.rearrange("(p t) l -> p t l", t=MT)[:, :, cols]
                             ).then_inc(w_in[half], 16)

            sp.dma_start(lw_rows[:], lora_weights.rearrange("(a i) -> a i", a=1).to_broadcast([P, NL])
                         ).then_inc(lw_in, 16)
            load_w(0)
            sp.dma_start(a_nat[:], lora_a.rearrange("i r l -> (i r) l")).then_inc(a_in, 16)
            load_w(1)
            load_first(0, QUARTER, x0_in[0])
            load_first(L - PAD, L, x0_edge_in)
            sp.wait_ge(toep_zero, 1)
            for s in range(TOEP_SP):
                load_toeplitz(sp, s, toep_in)
            sp.dma_start(cond_nat[:], cond).then_inc(cond_in, 16)
            sp.dma_start(ctxw_nat[:], ctx_w).then_inc(cond_in, 16)
            load_first(QUARTER, 2 * QUARTER, x0_in[1])
            sp.dma_start(chan_bias_rows[:], chan_bias.rearrange("(a m) -> a m", a=1).to_broadcast([P, C])
                         ).then_inc(chan_bias_in, 16)
            load_first(2 * QUARTER, 3 * QUARTER, x0_in[2])
            load_first(3 * QUARTER, L - PAD, x0_in[3])
            sp.dma_start(ffn_bias_rows[:], ffn_bias.rearrange("(a m) -> a m", a=1).to_broadcast([P, M])
                         ).then_inc(ffn_bias_in, 16)
            for g in range(1, GROUPS):
                if g > 1:
                    sp.wait_ge(x_in, 16 * (g - 1))
                sp.dma_start(xres[:, g * CG:(g + 1) * CG, :], x[:, g * CG:(g + 1) * CG, :]).then_inc(x_in, 16)

            def store(g, o, channels):
                sp.wait_ge(y_ready, nth(g, o + channels))
                sp.dma_start(out[:, bass.ds(nth(g, o), channels), :],
                             xres[:, bass.ds(nth(g, o), channels), :]).then_inc(out_done, 16)

            with sp.Fori(0, GROUPS - 1) as g:
                for o in range(0, CG, 2):
                    store(g, o, 2)
            for o in range(0, CG - 2, 2):
                store(GROUPS - 1, o, 2)
            store(GROUPS - 1, CG - 2, 1)
            for half in range(2):
                cols = slice(half * M // 2, (half + 1) * M // 2)
                sp.wait_ge(y_ready, C + half)
                sp.dma_start(out[:, C - 1, cols], xres[:, C - 1, cols]).then_inc(out_done, 16)
            sp.wait_ge(out_done, 16 * (C // 2 + 2))

        @block.gpsimd
        def _(pool):
            nc.gpsimd.memset(ident[:], 0.0).then_inc(ident_zero, 1)
            pool.wait_ge(ident_zero, 1)
            nc.gpsimd.affine_select(out=ident[:], in_=ident[:], compare_op=ALU.not_equal, fill=1.0, base=0,
                                    pattern=[[-1, P]], channel_multiplier=1).then_inc(ident_ready, 1)
            pool.wait_ge(toep_zero, 1)
            for s in range(TOEP_SP, S):
                load_toeplitz(pool, s, toep_in_pool)
            pool.wait_ge(ffn_bias_in, 16)

            PIECE = CG // 4

            def add_bias(g, i):
                part = xres[:, bass.ds(nth(g, PIECE * i), PIECE), :]
                nc.gpsimd.tensor_tensor(part, part, ffn_bias_rows[:].unsqueeze(1).to_broadcast([P, PIECE, M]),
                                        ALU.add).then_inc(xres_ready, 1)

            pool.wait_ge(xtile_ready, Q)
            for i in range(4):
                add_bias(0, i)
            with pool.Fori(1, GROUPS) as g:
                pool.wait_ge(xtile_ready, nth(g, Q))
                for i in reversed(range(4)):
                    add_bias(g, i)

        @block.scalar
        def _(act):
            act.dma_start(b_nat[:], lora_b.rearrange("i (p t) r -> p i t r", t=MT)).then_inc(b_in, 16)

            def xt_out(g, q):
                act.wait_ge(xt_ps, nth(g, q + 1))
                nc.scalar.copy(xt[:, q, :], ps_xt[:, q % 2, :]).then_inc(xt_ready, 1)

            def c_hi(g, o):
                act.wait_ge(ct_ps, nth(g, o + 1))
                nc.scalar.copy(ct_hi[:, o, :], ps_ct[:, o % 2, :]).then_inc(ct_hi_ready, 1)

            def w_hi(lt):
                act.wait_ge(weff_ready[lt], 1)
                nc.scalar.copy(wt_hi[:, lt, :], w_t[:, lt, :]).then_inc(wt_hi_ready[lt], 1)

            act.wait_ge(ident_ready, 1)
            nc.scalar.copy(table_scrap[:], ident[:, 0:1])
            for lt in range(KT - 1):
                w_out(act, nc.scalar.copy, lt)
            act.wait_ge(x0_in[0], 16)
            act.wait_ge(x0_edge_in, 16)
            order_x(act, nc.scalar.copy, 0, 0)
            order_x(act, nc.scalar.copy, 0, 1)
            xt_out(0, 0)
            xt_out(0, 1)
            act.wait_ge(cond_t_ps, 2)
            nc.scalar.copy(cond_t[:], ps_ct[:, 0, 0:P + C]).then_inc(cond_t_ready, 1)
            act.wait_ge(x0_in[1], 16)
            order_x(act, nc.scalar.copy, 0, 2)
            order_x(act, nc.scalar.copy, 0, 3)
            xt_out(0, 2)
            act.wait_ge(x0_in[2], 16)
            order_x(act, nc.scalar.copy, 0, 4)
            xt_out(0, 3)
            for q in range(4, Q):
                if q + 1 < Q:
                    if q + 1 == 3 * Q // 4:
                        act.wait_ge(x0_in[3], 16)
                    order_x(act, nc.scalar.copy, 0, q + 1)
                w_hi(q - 4)
                xt_out(0, q)
            for o in range(2):
                c_hi(0, o)
            with act.Fori(1, GROUPS) as g:
                act.wait_ge(x_in, 16 * g)
                order_x(act, nc.scalar.copy, g, 0)
                c_hi(g - 1, 2)
                xt_out(g, 0)
                order_x(act, nc.scalar.copy, g, 1)
                c_hi(g - 1, 3)
                c_hi(g - 1, 4)
                c_hi(g - 1, 5)
                xt_out(g, 1)
                order_x(act, nc.scalar.copy, g, 2)
                c_hi(g - 1, 6)
                c_hi(g - 1, 7)
                for q in range(2, Q - 1):
                    order_x(act, nc.scalar.copy, g, q + 1)
                    xt_out(g, q)
                xt_out(g, Q - 1)
                c_hi(g, 0)
                c_hi(g, 1)
            for o in range(2, CG):
                c_hi(GROUPS - 1, o)

        @block.vector
        def _(dve):
            def c_lo(g, o):
                dve.wait_ge(ct_hi_ready, nth(g, o + 1))
                nc.vector.tensor_tensor(ct_lo[:, o, :], ps_ct[:, o % 2, :],
                                        ct_hi[:, o, :].bitcast(F32), ALU.subtract).then_inc(ct_lo_ready, 1)

            def conv_out(g, q):
                dve.wait_ge(conv_ps, nth(g, q + 1))
                if q == 0:
                    wait_for(dve, ct_ps, nth(g, 0))
                nc.vector.tensor_tensor(
                    conv[:, :, q * CHUNK:(q + 1) * CHUNK],
                    ps_conv[:, q % 2, :].rearrange("p (l o) -> p o l", o=CG),
                    row_bias[:, bass.ds(g * CG, CG)].unsqueeze(2).to_broadcast([P, CG, CHUNK]),
                    ALU.add).then_inc(conv_ready, 1)

            def y_out(g, o):
                dve.wait_ge(y_ps, nth(g, o + 1))
                if o == 0:
                    dve.wait_ge(xres_ready, 4 * g + 4)
                row = xres[:, bass.ds(nth(g, o), 1), :].rearrange("p a m -> p (a m)")
                nc.vector.tensor_tensor(row, ps_y[:, o % 2, :], row, ALU.add).then_inc(y_ready, 1)

            def w_sum(lt):
                dve.wait_ge(lora_ps[lt], 1)
                dve.wait_ge(w_t_ready[lt], 1)
                nc.vector.tensor_tensor(w_t[:, lt, :], m_order(lora_bank(lt)), w_t[:, lt, :], ALU.add
                                        ).then_inc(weff_ready[lt], 1)

            def w_lo(lt):
                dve.wait_ge(wt_hi_ready[lt], 1)
                nc.vector.tensor_tensor(wt_lo[:, lt, :], w_t[:, lt, :], wt_hi[:, lt, :].bitcast(F32), ALU.subtract
                                        ).then_inc(wt_lo_ready[lt], 1)

            def forward(g, lo, hi):
                return toep_rev[:, g, :, J - hi:J - lo].rearrange("p o j -> p j o")[:, ::-1, :]

            nc.vector.memset(toep_rev[:], 0.0).then_inc(toep_zero, 1)
            nc.vector.memset(toep_wrap[:], 0.0).then_inc(toep_copied, 1)
            dve.wait_ge(b_in, 16)
            dve.wait_ge(lw_in, 16)
            for t in range(MT):
                nc.vector.tensor_tensor(b_col[:, t, :].rearrange("p (i r) -> p i r", i=NL), b_nat[:, :, t, :],
                                        lw_rows[:].unsqueeze(2).to_broadcast([P, NL, RANK]), ALU.mult
                                        ).then_inc(b_col_ready, 1)
            dve.wait_ge(bt_ps, 1)
            nc.vector.tensor_scalar(bt[:], ps_conv[:, 1, :], LORA_SCALE, None, ALU.mult).then_inc(bt_ready, 1)
            for lt in range(KT - 2):
                w_sum(lt)
            w_out(dve, nc.vector.tensor_copy, KT - 1)
            w_sum(KT - 2)
            dve.wait_ge(toep_in, 16 * TOEP_SP)
            dve.wait_ge(toep_in_pool, 16 * (S - TOEP_SP))
            for g in range(GROUPS):
                nc.vector.tensor_copy(toep_first[:, g, :, :], forward(g, 2 * PAD, J)).then_inc(toep_copied, 1)
                nc.vector.tensor_copy(toep[:, g, :, :], forward(g, 0, J)).then_inc(toep_copied, 1)
                dve.wait_ge(toep_copied, 2 * g + 3)
                edge_cleared = nc.vector.memset(toep_first[0:EDGE, g, :, :], 0.0)
                if g == 0:
                    edge_cleared.then_inc(toep_ready, 1)
                    w_sum(KT - 1)
            nc.vector.tensor_copy(toep_wrap[0:EDGE], toep[0:EDGE, :, 0:2 * PAD, :]).then_inc(toep_ready, 1)
            dve.wait_ge(ctx_ps, 1)
            dve.wait_ge(chan_bias_in, 16)
            nc.vector.tensor_tensor(row_bias[:], ps_ct[:, 1, 0:C], chan_bias_rows[:], ALU.add
                                    ).then_inc(row_bias_ready, 1)
            dve.wait_ge(row_bias_ready, 1)
            for q in range(Q):
                conv_out(0, q)
                if Q - 1 - KT <= q < Q - 1:
                    w_lo(q - (Q - 1 - KT))
            for o in range(2):
                c_lo(0, o)
            with dve.Fori(1, GROUPS) as g:
                y_out(g - 1, 0)
                c_lo(g - 1, 2)
                c_lo(g - 1, 3)
                y_out(g - 1, 1)
                c_lo(g - 1, 4)
                c_lo(g - 1, 5)
                y_out(g - 1, 2)
                c_lo(g - 1, 6)
                c_lo(g - 1, 7)
                y_out(g - 1, 3)
                conv_out(g, 0)
                conv_out(g, 1)
                y_out(g - 1, 4)
                conv_out(g, 2)
                conv_out(g, 3)
                y_out(g - 1, 5)
                conv_out(g, 4)
                conv_out(g, 5)
                conv_out(g, 6)
                conv_out(g, 7)
                y_out(g - 1, 6)
                c_lo(g, 0)
                y_out(g - 1, 7)
                c_lo(g, 1)
            last = GROUPS - 1
            for o in range(CG - 1):
                y_out(last, o)
                if o + 2 < CG:
                    c_lo(last, o + 2)
            for half in range(2):
                cols = slice(half * M // 2, (half + 1) * M // 2)
                dve.wait_ge(y_ps, C + half)
                nc.vector.tensor_tensor(xres[:, C - 1, cols], ps_y[:, 1 - half, cols], xres[:, C - 1, cols], ALU.add
                                        ).then_inc(y_ready, 1)

        @block.tensor
        def _(pe):
            def transpose_x(g, q):
                n = nth(g, q)
                pe.wait_ge(xtile_ready, n + 1)
                wait_for(pe, xt_ready, n - 1)
                for t in range(TPC):
                    mm = nc.tensor.transpose(ps_xt[:, q % 2, t * P:(t + 1) * P], xtile[:, q % RING, t, :], ident[:])
                mm.then_inc(xt_ps, 1)

            def convolve(g, q):
                n = nth(g, q)
                pe.wait_ge(xt_ready, nth(g, min(q + 2, Q)))
                wait_for(pe, conv_ready, n - 1)

                def product(slot, tile, matrix, lo, hi, start=False):
                    return nc.tensor.matmul(ps_conv[:, q % 2, lo * CG:hi * CG], xt[:, slot, tile * P:(tile + 1) * P],
                                            matrix.rearrange("p a j o -> p (a j o)"),
                                            start=start, stop=False, skip_group_check=True)

                here = bass.ds(g, 1)
                if q == 0:
                    product(q, 0, toep_first[:, here, :, :], 0, J - 2 * PAD, start=True)
                else:
                    product(q, 0, toep[:, here, 2 * PAD:J, :], 0, J - 2 * PAD, start=True)
                for t in range(1, TPC):
                    product(q, t, toep[:, here, :, :], t * S - 2 * PAD, t * S - 2 * PAD + J)
                if q < Q - 1:
                    mm = product(q + 1, 0, toep[:, here, 0:2 * PAD, :], CHUNK - 2 * PAD, CHUNK)
                else:
                    mm = product(0, 0, toep_wrap[:, here, :, :], CHUNK - 2 * PAD, CHUNK)
                mm.then_inc(conv_ps, 1)

            def transpose_conv(g, o, lts=range(KT)):
                n = nth(g, o)
                if 0 in lts:
                    wait_for(pe, ct_lo_ready, n - 1)
                for lt in lts:
                    if o == 0 and lt == 0:
                        pe.wait_ge(conv_ready, nth(g, Q - Q // KT))
                    if o == 0 and lt == KT - 1:
                        pe.wait_ge(conv_ready, nth(g, Q))
                    mm = nc.tensor.transpose(ps_ct[:, o % 2, lt * P:(lt + 1) * P],
                                             conv[:, o, lt * P:(lt + 1) * P], ident[:])
                if KT - 1 in lts:
                    mm.then_inc(ct_ps, 1)

            def ffn(g, o):
                n = nth(g, o)
                pe.wait_ge(ct_hi_ready, n + 1)
                if o == 1:
                    pe.wait_ge(ct_lo_ready, n + 1)
                if o > 1:
                    pe.wait_ge(y_ready, n - 1)
                for ct, wt in ((ct_hi, wt_hi), (ct_hi, wt_lo), (ct_lo, wt_hi)):
                    if ct is ct_lo:
                        pe.wait_ge(ct_lo_ready, n + 1)
                    for lt in range(KT):
                        mm = nc.tensor.matmul(ps_y[:, o % 2, :], ct[:, o, lt * P:(lt + 1) * P], wt[:, lt, :],
                                              start=(lt == 0 and ct is ct_hi and wt is wt_hi),
                                              stop=(lt == KT - 1 and ct is ct_lo))
                mm.then_inc(y_ps, 1)

            pe.wait_ge(ident_ready, 1)
            for _ in range(WARM_UP):
                nc.tensor.matmul(ps_conv[:, 0, 0:P], ident[:], ident[:], start=True, stop=True)
            pe.wait_ge(b_col_ready, MT)
            for t in range(MT):
                mm = nc.tensor.transpose(ps_conv[:, 1, t * P:(t + 1) * P], b_col[:, t, :], ident[:])
            mm.then_inc(bt_ps, 1)

            def transpose_w(lt):
                for t in range(MT):
                    mm = nc.tensor.transpose(w_bank(lt)[:, t * P:(t + 1) * P], w_nat[:, t, lt * P:(lt + 1) * P],
                                             ident[:])
                mm.then_inc(w_ps[lt], 1)

            def lora(lt):
                nc.tensor.matmul(lora_bank(lt), a_nat[:, lt * P:(lt + 1) * P], bt[:], start=True, stop=True
                                 ).then_inc(lora_ps[lt], 1)

            pe.wait_ge(w_in[0], 16)
            transpose_w(0)
            transpose_w(1)
            pe.wait_ge(a_in, 16)
            pe.wait_ge(bt_ready, 1)
            lora(0)
            lora(1)
            pe.wait_ge(w_in[1], 16)
            transpose_w(2)
            transpose_w(3)
            pe.wait_ge(w_t_ready[0], 1)
            lora(2)
            for q in range(2):
                pe.wait_ge(w_t_ready[q + 2], 1)
                transpose_x(0, q)
            pe.wait_ge(w_t_ready[1], 1)
            lora(3)
            pe.wait_ge(cond_in, 32)
            pe.wait_ge(weff_ready[0], 1)
            nc.tensor.transpose(ps_ct[:, 0, 0:P], cond_nat[:], ident[:]).then_inc(cond_t_ps, 1)
            nc.tensor.transpose(ps_ct[:, 0, P:P + C], ctxw_nat[:], ident[0:C, 0:C]).then_inc(cond_t_ps, 1)
            pe.wait_ge(toep_ready, 1)
            convolve(0, 0)
            transpose_x(0, 2)
            pe.wait_ge(cond_t_ready, 1)
            pe.wait_ge(weff_ready[1], 1)
            nc.tensor.matmul(ps_ct[:, 1, 0:C], cond_t[:, 0:P], cond_t[:, P:P + C], start=True, stop=True
                             ).then_inc(ctx_ps, 1)
            transpose_x(0, 3)
            convolve(0, 1)
            for q in range(4, Q):
                transpose_x(0, q)
                convolve(0, q - 2)
            pe.wait_ge(toep_ready, 2)
            convolve(0, Q - 2)
            convolve(0, Q - 1)
            pe.wait_ge(row_bias_ready, 1)
            for o in range(2):
                transpose_conv(0, o, range(KT - 1))
            for o in range(2):
                transpose_conv(0, o, range(KT - 1, KT))
            for lt in range(KT):
                pe.wait_ge(wt_lo_ready[lt], 1)
            with pe.Fori(1, GROUPS) as g:
                ffn(g - 1, 0)
                transpose_conv(g - 1, 2)
                transpose_x(g, 0)
                transpose_conv(g - 1, 3)
                ffn(g - 1, 1)
                transpose_conv(g - 1, 4)
                transpose_conv(g - 1, 5)
                transpose_x(g, 1)
                ffn(g - 1, 2)
                transpose_conv(g - 1, 6)
                transpose_conv(g - 1, 7)
                ffn(g - 1, 3)
                transpose_x(g, 2)
                convolve(g, 0)
                transpose_x(g, 3)
                convolve(g, 1)
                ffn(g - 1, 4)
                transpose_x(g, 4)
                convolve(g, 2)
                transpose_x(g, 5)
                convolve(g, 3)
                ffn(g - 1, 5)
                transpose_x(g, 6)
                convolve(g, 4)
                transpose_x(g, 7)
                convolve(g, 5)
                convolve(g, 6)
                convolve(g, 7)
                ffn(g - 1, 6)
                transpose_conv(g, 0)
                ffn(g - 1, 7)
                transpose_conv(g, 1)
                pe.wait_ge(y_ready, nth(g - 1, CG - 1))
            last = GROUPS - 1
            for o in range(CG - 1):
                ffn(last, o)
                if o + 2 < CG:
                    transpose_conv(last, o + 2)
            pe.wait_ge(ct_lo_ready, C)
            for half in range(2):
                cols = slice(half * M // 2, (half + 1) * M // 2)
                pe.wait_ge(y_ready, C - 2 + half)
                for ct, wt in ((ct_hi, wt_hi), (ct_hi, wt_lo), (ct_lo, wt_hi)):
                    for lt in range(KT):
                        mm = nc.tensor.matmul(ps_y[:, 1 - half, cols], ct[:, CG - 1, lt * P:(lt + 1) * P],
                                              wt[:, lt, cols], start=(lt == 0 and ct is ct_hi and wt is wt_hi),
                                              stop=(lt == KT - 1 and ct is ct_lo))
                mm.then_inc(y_ps, 1)


_INS = ['x', 'cond_128', 'fside_S_0', 'L0_cond_weight', 'L0_cond_c_weight', 'L0_ffn_lora_A', 'L0_ffn_lora_B',
        'L0_ffn_W', 'L0_ffn_bias', 'L0_ffn_lora_weights']
_OUTS = [((128, 32, 512), 'float32')]


def kernel(**inputs):
    import numpy as _np
    import concourse.bacc as _bacc
    from concourse import mybir as _mybir
    from concourse.bass_utils import run_bass_kernel_spmd as _run

    nc = _bacc.Bacc("TRN2", target_bir_lowering=False, num_devices=1)
    arrays, args = {}, []
    for name in _INS:
        a = _np.ascontiguousarray(inputs[name])
        arrays[f"in_{name}_dram"] = a
        args.append(nc.dram_tensor(f"in_{name}_dram", a.shape, _mybir.dt.from_np(a.dtype), kind="ExternalInput").ap())
    for i, (shape, dtype) in enumerate(_OUTS):
        dt = _mybir.dt.from_np(_np.dtype(dtype))
        args.append(nc.dram_tensor(f"out_{i}_dram", shape, dt, kind="ExternalOutput").ap())
    adaln_ffn(nc, *args)
    r = _run(nc, [arrays], core_ids=[0])
    got = tuple(r.results[0][f"out_{i}_dram"] for i in range(len(_OUTS)))
    return got[0]
```
